# Optimizing a Trainium2 kernel written in Bass

```python
import numpy as np
import jax
import jax.numpy as jnp

def _softmax(x, axis=-1):
    return jax.nn.softmax(x, axis=axis)

def _gelu(x):
    return jax.nn.gelu(x, approximate=True)

def _silu(x):
    return jax.nn.silu(x)

def _sigmoid(x):
    return jax.nn.sigmoid(x)

def _layernorm(x, axis=-1, eps=1e-05):
    m = jnp.mean(x, axis=axis, keepdims=True)
    v = jnp.var(x, axis=axis, keepdims=True)
    return (x - m) / jnp.sqrt(v + eps)

def _scatter_add(tgt, idx, src, axis=0):
    return tgt.at[idx].add(src)

def _segment_sum(src, seg, n):
    return jax.ops.segment_sum(src, seg, n)
kernel_name = 'mk_flamingo_gated_d1_seqx_r8_37eb9a'

def setup_inputs(seed: int=0):
    np.random.seed(seed)
    _w = jnp.asarray

    def _rec_inputs():
        import jax
        import jax.numpy as jnp
        _rk = jax.random.key(seed)
        x = -0.0002928 + 1 * jax.random.normal(jax.random.fold_in(_rk, 1), (8, 100, 128), jnp.float32)
        _lenS = 100 - jax.random.randint(jax.random.fold_in(_rk, 7), (8,), 0, max(1, 100 // 4) + 1, jnp.int32)
        _lenS2 = 1444 - jax.random.randint(jax.random.fold_in(_rk, 8), (8,), 0, max(1, 1444 // 4) + 1, jnp.int32)
        _ctx_512P = jax.random.normal(jax.random.fold_in(_rk, 11), (8, 16, 64), jnp.float32)
        _ctx_512c = jax.random.dirichlet(jax.random.fold_in(_rk, 511), 0.3 * jnp.ones((16,), jnp.float32), (8, 1444))
        _ctx_512t = jnp.einsum('bsk,bkd->bsd', _ctx_512c, _ctx_512P)
        _ctx_512t = _ctx_512t * jax.lax.rsqrt(jnp.mean(jnp.square(_ctx_512t)) + 1e-12) * 0.953939
        ctx_512 = -1.52775e-05 + 0.999936 * (_ctx_512t + 0.3 * jax.random.normal(jax.random.fold_in(_rk, 611), (8, 1444, 64), jnp.float32))
        _g = jax.random.normal(jax.random.fold_in(_rk, 9001), (2, 1), jnp.float32)
        _g = jnp.sign(_g) * jnp.maximum(jnp.abs(_g), 1.0) + (_g == 0) * 1.0
        g_xattn = _g[0]
        g_ffn = _g[1]
        return (x, ctx_512, g_xattn, g_ffn)
    x, ctx_512, g_xattn, g_ffn = _rec_inputs()

    def _L0_xattn_setup():
        import jax, jax.numpy as jnp
        import numpy as np
        NUM_HEADS = 16
        HEAD_DIM = 64
        Q_DIM = 128
        KV_DIM = 64
        INNER = NUM_HEADS * HEAD_DIM
        key = jax.random.key(seed)
        ks = jax.random.split(key, 7)
        B, N, M = (32, 128, 256)
        q = jax.random.normal(ks[0], (B, N, Q_DIM), dtype=jnp.float32)
        kv = jax.random.normal(ks[1], (B, M, KV_DIM), dtype=jnp.float32)
        Wq = jax.random.normal(ks[2], (Q_DIM, INNER), dtype=jnp.float32) / np.sqrt(Q_DIM)
        Wk = jax.random.normal(ks[3], (KV_DIM, INNER), dtype=jnp.float32) / np.sqrt(KV_DIM)
        Wv = jax.random.normal(ks[4], (KV_DIM, INNER), dtype=jnp.float32) / np.sqrt(KV_DIM)
        Wo = jax.random.normal(ks[5], (INNER, Q_DIM), dtype=jnp.float32) / np.sqrt(INNER)
        bo = jax.random.normal(ks[6], (Q_DIM,), dtype=jnp.float32) * 0.01
        return {'q': q, 'kv': kv, 'Wq': Wq, 'Wk': Wk, 'Wv': Wv, 'Wo': Wo, 'bo': bo}
    _L0_xattn_all = _L0_xattn_setup()
    _L0_xattn_in = {k: v for k, v in _L0_xattn_all.items() if k in ('Wq', 'Wk', 'Wv', 'Wo', 'bo')}
    del _L0_xattn_all

    def _L0_ffn_setup():
        import jax, jax.numpy as jnp
        import numpy as np
        BLOCK = 16
        _GRID = jnp.array([0.0, 0.5, 1.0, 1.5, 2.0, 3.0, 4.0, 6.0], dtype=jnp.float32)
        _MID = jnp.array([0.25, 0.75, 1.25, 1.75, 2.5, 3.5, 5.0], dtype=jnp.float32)

        def fp4_quant_dequant(x):
            shape = x.shape
            xb = x.reshape(shape[:-1] + (shape[-1] // BLOCK, BLOCK))
            scale = jnp.max(jnp.abs(xb), axis=-1, keepdims=True) / 6.0
            scale = jnp.maximum(scale, jnp.float32(1e-12))
            xn = xb / scale
            idx = jnp.searchsorted(_MID, jnp.abs(xn))
            q = _GRID[idx] * jnp.sign(xn) * scale
            return q.reshape(shape)

        def fp4_linear(x, w):
            xq = fp4_quant_dequant(x)
            wq = fp4_quant_dequant(w)
            return jnp.einsum('bsk,nk->bsn', xq, wq)
        key = jax.random.key(seed)
        k1, k2, k3, k4 = jax.random.split(key, 4)
        H, I = (128, 352)
        x = jax.random.normal(k1, (4, 512, H), dtype=jnp.float32)
        w_gate = jax.random.normal(k2, (I, H), dtype=jnp.float32) * 0.02
        w_up = jax.random.normal(k3, (I, H), dtype=jnp.float32) * 0.02
        w_down = jax.random.normal(k4, (H, I), dtype=jnp.float32) * 0.02
        return {'x': x, 'w_gate': w_gate, 'w_up': w_up, 'w_down': w_down}
    _L0_ffn_all = _L0_ffn_setup()
    _L0_ffn_in = {k: v for k, v in _L0_ffn_all.items() if k in ('w_gate', 'w_up', 'w_down')}
    del _L0_ffn_all
    return {'x': x, 'ctx_512': ctx_512, 'g_xattn': g_xattn, 'g_ffn': g_ffn, 'L0_xattn_Wq': _L0_xattn_in['Wq'], 'L0_xattn_Wk': _L0_xattn_in['Wk'], 'L0_xattn_Wv': _L0_xattn_in['Wv'], 'L0_xattn_Wo': _L0_xattn_in['Wo'], 'L0_xattn_bo': _L0_xattn_in['bo'], 'L0_ffn_w_gate': _L0_ffn_in['w_gate'], 'L0_ffn_w_up': _L0_ffn_in['w_up'], 'L0_ffn_w_down': _L0_ffn_in['w_down']}

def reference(x, ctx_512, g_xattn, g_ffn, L0_xattn_Wq, L0_xattn_Wk, L0_xattn_Wv, L0_xattn_Wo, L0_xattn_bo, L0_ffn_w_gate, L0_ffn_w_up, L0_ffn_w_down):
    import jax
    import jax.numpy as jnp

    def _L0_xattn_ref(q, kv, Wq, Wk, Wv, Wo, bo):
        import jax, jax.numpy as jnp
        import numpy as np
        NUM_HEADS = 16
        HEAD_DIM = 64
        Q_DIM = 128
        KV_DIM = 64
        INNER = NUM_HEADS * HEAD_DIM
        B, N, _ = q.shape
        M = kv.shape[1]
        scale = HEAD_DIM ** (-0.5)
        qh = (q @ Wq).reshape(B, N, NUM_HEADS, HEAD_DIM).transpose(0, 2, 1, 3)
        kh = (kv @ Wk).reshape(B, M, NUM_HEADS, HEAD_DIM).transpose(0, 2, 1, 3)
        vh = (kv @ Wv).reshape(B, M, NUM_HEADS, HEAD_DIM).transpose(0, 2, 1, 3)
        scores = jnp.einsum('bhnd,bhmd->bhnm', qh, kh) * scale
        attn = jax.nn.softmax(scores, axis=-1)
        out = jnp.einsum('bhnm,bhmd->bhnd', attn, vh)
        out = out.transpose(0, 2, 1, 3).reshape(B, N, INNER)
        return out @ Wo + bo

    def _L0_ffn_ref(x, w_gate, w_up, w_down):
        import jax, jax.numpy as jnp
        import numpy as np
        BLOCK = 16
        _GRID = jnp.array([0.0, 0.5, 1.0, 1.5, 2.0, 3.0, 4.0, 6.0], dtype=jnp.float32)
        _MID = jnp.array([0.25, 0.75, 1.25, 1.75, 2.5, 3.5, 5.0], dtype=jnp.float32)

        def fp4_quant_dequant(x):
            shape = x.shape
            xb = x.reshape(shape[:-1] + (shape[-1] // BLOCK, BLOCK))
            scale = jnp.max(jnp.abs(xb), axis=-1, keepdims=True) / 6.0
            scale = jnp.maximum(scale, jnp.float32(1e-12))
            xn = xb / scale
            idx = jnp.searchsorted(_MID, jnp.abs(xn))
            q = _GRID[idx] * jnp.sign(xn) * scale
            return q.reshape(shape)

        def fp4_linear(x, w):
            xq = fp4_quant_dequant(x)
            wq = fp4_quant_dequant(w)
            return jnp.einsum('bsk,nk->bsn', xq, wq)
        gate = fp4_linear(x, w_gate)
        y = fp4_linear(x, w_up)
        h = jax.nn.silu(gate) * y
        return fp4_linear(h, w_down)
    x = x + jnp.tanh(g_xattn[0]) * _L0_xattn_ref(_layernorm(x, axis=-1), ctx_512, L0_xattn_Wq, L0_xattn_Wk, L0_xattn_Wv, L0_xattn_Wo, L0_xattn_bo)
    x = x + jnp.tanh(g_ffn[0]) * _L0_ffn_ref(_layernorm(x, axis=-1), L0_ffn_w_gate, L0_ffn_w_up, L0_ffn_w_down)
    return x

_drawn_inputs = setup_inputs


def setup_inputs(seed=0):
    import zlib

    import numpy as np

    out = dict(_drawn_inputs(seed))
    spreads = {}
    factors = {'L0_xattn_bo': 7.507, 'L0_ffn_w_gate': 6.028, 'L0_ffn_w_up': 5.555, 'L0_ffn_w_down': 5.532}
    for name, (base, spread) in spreads.items():
        noise = np.random.default_rng([zlib.crc32(name.encode()), seed]).standard_normal(out[name].shape)
        drawn = base * np.exp(spread * noise) if base else spread * noise
        out[name] = jnp.asarray(drawn.astype(out[name].dtype))
    for name, factor in factors.items():
        out[name] = (out[name] * factor).astype(out[name].dtype)
    return out
```

```python
from contextlib import ExitStack

import concourse.bass as bass
from concourse import mybir

F32 = mybir.dt.float32
F32R = mybir.dt.float32r
I32 = mybir.dt.int32
ALU = mybir.AluOpType
ACT = mybir.ActivationFunctionType
AX = mybir.AxisListType

B, N, D = 8, 100, 128
M, C = 1444, 64
H = 16
INNER = H * C
F = 352
BLOCK = 16
HG = H // 2
ROWS = HG * N
HALF = ROWS // 2
GROUPS = 2 * B
CHUNKS = 12
PFULL = M // CHUNKS
EXTRA = M - PFULL * CHUNKS
CROWS = [PFULL + (c < EXTRA) for c in range(CHUNKS)]
COFF = [sum(CROWS[:c]) for c in range(CHUNKS + 1)]
TILES, TROWS = 7, 116
TSIZE = [min(TROWS, ROWS - t * TROWS) for t in range(TILES)]
MAXC = [0, 482, 964, M]
KS1 = 6
EPS = 1e-5
SGN = -2147483648
FT = [128, 128, 96]
WALL = 3 * D + 3 * D + F
LINKS = 15

MAX_STEPS = {2: 3, 3: 3, 4: 2, 5: 2, 6: 3, 7: 3, 8: 3, 9: 2}


def ring_keys(g, step):
    keys = []
    pre = g + 1 < GROUPS
    if pre and step == 0:
        keys += [("q", 0), ("q", 1)]
    if g == 0 and step == 1:
        keys += [("wvT", 0)]
    if g == 0 and 3 <= step <= 6:
        keys += [("vo", step - 3)]
    if g == 1:
        keys += {0: [("wT", 0)], 1: [("wT", 1)], 2: [("wT", 2)], 9: [("wT", 3)], 11: [("wT", 4)]}.get(step, [])
    if g % 2 and g >= 3:
        keys += {0: [("zT", 0)], 1: [("gate", 0)], 2: [("up", 0)], 9: [("hT", 0)], 11: [("down", 0)]}.get(step, [])
    if g % 2 and pre and step == 1:
        keys += [("ctx", k) for k in range(3)]
    if g >= 1:
        keys += {2: [("sum", 0)], 4: [("proj", 0)], 5: [("proj", 1)]}.get(step, [])
    if g % 2 == 0 and g + 2 < GROUPS and step == 6:
        keys += [("xT", 0)]
    if pre and step in MAX_STEPS:
        u0 = sum(n for s, n in MAX_STEPS.items() if s < step)
        keys += [("max", u) for u in range(u0, u0 + MAX_STEPS[step])]
    if pre and step == 10:
        keys += [("shift", 0)]
    return keys


START = ([("wqT", 0), ("wqT", 1), ("wkT", 0), ("ctx", 0), ("ctx", 1), ("ctx", 2), ("xT", 0), ("A", 0), ("A", 1),
          ("q", 0), ("q", 1)] + [("max", u) for u in range(21)] + [("shift", 0)])
FINISH = [("sum", 0), ("proj", 0), ("proj", 1), ("zT", 0), ("gate", 0), ("up", 0), ("hT", 0), ("down", 0)]


def number_ring():
    index, n = {}, 0
    for key in START:
        index[(-1, key)] = n
        n += 1
    for g in range(GROUPS):
        for step in range(CHUNKS):
            for key in ring_keys(g, step):
                index[(g, key)] = n
                n += 1
    for key in FINISH:
        index[(GROUPS, key)] = n
        n += 1
    return index


RING = number_ring()
RING_PER_LOOP = RING[(6, ("q", 0))] - RING[(2, ("q", 0))]
assert RING_PER_LOOP % 2 == 0
for _g in range(1, 10):
    for _s in range(CHUNKS):
        for _k in ring_keys(_g, _s):
            if _k[0] != "wT":
                assert RING[(_g + 4, _k)] - RING[(_g, _k)] == RING_PER_LOOP


class Turn:

    def __init__(self, g, p=0):
        self.g, self.p = g, p

    def count(self, per_group, plus):
        return per_group * self.g + plus + (4 * per_group) * self.p

    def batch(self, ahead=0):
        return self.g // 2 + ahead + 2 * self.p

    def parity(self, ahead=0):
        return (self.g // 2 + ahead) % 2

    def fills(self, ahead=0):
        return (self.g // 2 + ahead) // 2 + 1 + self.p

    def ring(self, key):
        i = RING[(self.g, key)]
        assert self.g >= 1 or isinstance(self.p, int)
        return i % 2, i // 2 + 1 + (RING_PER_LOOP // 2) * self.p

    def before(self):
        return Turn(self.g - 1, self.p)


def xattn_ffn(nc, x, ctx_in, g_xattn, g_ffn, Wq, Wk, Wv, Wo, bo, w_gate, w_up, w_down, out):
    with ExitStack() as es:
        def sb(name, shape, dt=F32):
            return es.enter_context(nc.sbuf_tensor(name, shape, dt))

        def sem(name):
            return es.enter_context(nc.semaphore(name))

        scores = es.enter_context(nc.psum_tensor("scores", [128, 2, 2, 512], F32))
        attn = es.enter_context(nc.psum_tensor("attn", [128, 2, 512], F32))
        ring = es.enter_context(nc.psum_tensor("ring", [128, 2, 512], F32))

        ident = sb("ident", [128, 128])
        ones = sb("ones", [128, 2])
        minus_half = sb("minus_half", [128, 1])
        eps = sb("eps", [128, 1])
        unused = sb("unused", [128, 1])
        shift_mask = sb("shift_mask", [128, TILES, TROWS])
        tanh_x = sb("tanh_x", [128, 1])
        tanh_f = sb("tanh_f", [128, 1])
        bo_bc = sb("bo_bc", [128, D])
        wq = sb("wq", [128, INNER])
        wk = sb("wk", [C, INNER])
        wv = sb("wv", [C, INNER])
        wo = sb("wo", [128, HG, D])
        wqT = sb("wqT", [128, HG, D])
        wkT = sb("wkT", [128, HG, C])
        wvT = sb("wvT", [128, HG, 2, C])
        a_dup = sb("a_dup", [128, H, 2, C])
        vo = sb("vo", [128, H, D])
        w_raw = sb("w_raw", [128, WALL])
        w_fp4 = sb("w_fp4", [128, WALL])
        w_abs = sb("w_abs", [128, WALL])
        w_t = sb("w_t", [128, WALL])
        w_small = sb("w_small", [128, 2, WALL // BLOCK])
        gateT = sb("gateT", [128, F])
        upT = sb("upT", [128, F])
        downT = sb("downT", [128, 3, D])
        ctx_n = sb("ctx_n", [128, 2, CHUNKS, 2, C])
        k_hl = [sb(f"k_hl{i}", [128, M], F32R) for i in range(2)]
        k_h1 = [sb(f"k_h1{i}", [128, M], F32R) for i in range(2)]
        q_hh = sb("q_hh", [128, 2, ROWS], F32R)
        q_ls = sb("q_ls", [128, 2, TILES * TROWS], F32R)
        max3 = sb("max3", [128, TILES, 3])
        maxes = sb("maxes", [128, TILES])
        probs = sb("probs", [128, KS1, ROWS])
        acc_v = sb("acc_v", [128, 2, ROWS])
        acc_p = sb("acc_p", [128, 2, ROWS])
        attn_sb = sb("attn_sb", [128, ROWS])
        rsum = sb("rsum", [128, HG])
        x_in = sb("x_in", [128, 2, D])
        x_res = sb("x_res", [128, 2, D])
        x_hat = sb("x_hat", [128, D])
        xT = sb("xT", [128, 2, N])
        y = sb("y", [128, 2, D])
        stats = sb("stats", [128, 2, 8])
        rstd = sb("rstd", [128, 2])
        z = sb("z", [128, D])
        z_fp4 = sb("z_fp4", [128, D])
        zT = sb("zT", [128, N])
        e_gate = sb("e_gate", [128, F])
        hid = sb("hid", [128, F])
        h_fp4 = sb("h_fp4", [128, F])
        hT = sb("hT", [128, 3, N])
        f_abs = sb("f_abs", [128, F])
        f_t = sb("f_t", [128, F])
        f_small = sb("f_small", [128, 2, F // BLOCK])
        y_out = sb("y_out", [128, 2, D])

        wqk_in = sem("wqk_in")
        wvo_in = sem("wvo_in")
        ffn_in = sem("ffn_in")
        small_in = sem("small_in")
        x_loaded = [sem(f"x_loaded{i}") for i in range(2)]
        ctx_loaded = [sem(f"ctx_loaded{i}") for i in range(2)]
        consts_set = sem("consts_set")
        consts_v = sem("consts_v")
        gates_set = sem("gates_set")
        ring_full = [sem(f"ring_full{i}") for i in range(2)]
        ring_free = [sem(f"ring_free{i}") for i in range(2)]
        q_hi_done = sem("q_hi_done")
        k_hi_done = sem("k_hi_done")
        max_done = sem("max_done")
        scores_full = sem("scores_full")
        probs_full = sem("probs_full")
        pv_done = sem("pv_done")
        attn_copied = sem("attn_copied")
        sum_v = sem("sum_v")
        sum_p = sem("sum_p")
        norm_done = sem("norm_done")
        head_done = sem("head_done")
        ln1_stats = sem("ln1_stats")
        ln1_eps = sem("ln1_eps")
        ln1_rstd = sem("ln1_rstd")
        ln1_done = sem("ln1_done")
        res_done = sem("res_done")
        tbo_done = sem("tbo_done")
        ln2_stats = sem("ln2_stats")
        ln2_eps = sem("ln2_eps")
        ln2_rstd = sem("ln2_rstd")
        ln2_done = sem("ln2_done")
        wq4 = sem("wq4")
        zq4 = sem("zq4")
        hq4 = sem("hq4")
        e_done = sem("e_done")
        hid_done = sem("hid_done")
        stored = [sem(f"stored{i}") for i in range(2)]

        block = es.enter_context(nc.Block())

        def wait_reads(engine, *uses, own=None):
            last = {}
            for t, key in uses:
                bank, n = t.ring(key)
                if bank != own and (bank not in last or RING[(t.g, key)] > last[bank][0]):
                    last[bank] = (RING[(t.g, key)], n)
            for bank, (_, n) in last.items():
                engine.wait_ge(ring_free[bank], n)

        def all_groups(engine, group, finish):
            for g in (0, 1):
                group(Turn(g))
            with engine.Fori(0, (GROUPS - 4) // 4) as p:
                for g in (2, 3, 4, 5):
                    group(Turn(g, p))
            for g in (GROUPS - 2, GROUPS - 1):
                group(Turn(g))
            finish(Turn(GROUPS))

        @block.sync
        def _(sp):
            def load_ctx(b, par):
                for i in range(2):
                    sp.dma_start(ctx_n[0:PFULL, par, :, i, :], ctx_in[b, 0:PFULL * CHUNKS, :].rearrange("(p c) d -> p c d", c=CHUNKS)).then_inc(ctx_loaded[par], 16)
                    sp.dma_start(ctx_n[PFULL:PFULL + 1, par, 0:EXTRA, i, :], ctx_in[b, PFULL * CHUNKS:M, :].rearrange("(p c) d -> p c d", c=EXTRA)).then_inc(ctx_loaded[par], 16)

            def load_x(b, par):
                sp.dma_start(x_in[0:N, par, :], x[b, :, :]).then_inc(x_loaded[par], 16)

            sp.dma_start(wq[:, :], Wq).then_inc(wqk_in, 16)
            sp.dma_start(wk[:, :], Wk).then_inc(wqk_in, 16)
            load_ctx(0, 0)
            load_x(0, 0)
            sp.dma_start(tanh_x[:, :], g_xattn.partition_broadcast(128)).then_inc(small_in, 16)
            sp.dma_start(tanh_f[:, :], g_ffn.partition_broadcast(128)).then_inc(small_in, 16)
            sp.dma_start(bo_bc[:, :], bo.partition_broadcast(128)).then_inc(small_in, 16)
            sp.dma_start(wv[:, :], Wv).then_inc(wvo_in, 16)
            sp.dma_start(wo[:, :, :], Wo.rearrange("(j p) n -> p j n", p=128)).then_inc(wvo_in, 16)
            sp.wait_ge(consts_v, 1)
            for i, w in enumerate((w_gate, w_up)):
                at = w_raw[:, i * 3 * D:(i + 1) * 3 * D].rearrange("p (k n) -> p k n", k=3)
                sp.dma_start(at[:, 0:2, :], w[0:256, :].rearrange("(k p) n -> p k n", p=128)).then_inc(ffn_in, 16)
                sp.dma_start(at[0:FT[2], 2, :], w[256:F, :]).then_inc(ffn_in, 16)
            sp.dma_start(w_raw[:, 6 * D:], w_down).then_inc(ffn_in, 16)

            def store(t):
                b, par = t.batch(-1), t.parity(-1)
                wait_reads(sp, (t, ("down", 0)))
                sp.dma_start(out[b, :, :], y_out[0:N, par, :]).then_inc(stored[par], 16)

            def group(t):
                if t.g % 2 == 0 and t.g + 2 < GROUPS:
                    if t.g >= 2:
                        sp.wait_ge(res_done, t.batch())
                        sp.wait_ge(ln1_done, t.batch())
                    load_x(t.batch(1), t.parity(1))
                    if t.g >= 2:
                        sp.wait_ge(pv_done, t.count(6, 0))
                    load_ctx(t.batch(1), t.parity(1))
                if t.g % 2 and t.g >= 3:
                    store(t)

            def finish(t):
                store(t)
                for par in range(2):
                    sp.wait_ge(stored[par], 16 * (B // 2 + 1))

            all_groups(sp, group, finish)

        @block.gpsimd
        def _(pool):
            pool.memset(ident[:, :], 0.0).then_inc(consts_set, 1)
            pool.memset(shift_mask[:, :, :], 0.0).then_inc(consts_set, 1)
            pool.memset(ones[:, :], 1.0).then_inc(consts_set, 1)
            pool.memset(minus_half[:, :], -0.5).then_inc(consts_set, 1)
            pool.memset(eps[:, :], EPS).then_inc(consts_set, 1)
            for par in range(2):
                pool.memset(y_out[:, par, :], 0.0).then_inc(stored[par], 16)
            pool.wait_ge(consts_set, 5)
            pool.affine_select(out=ident[:, :], in_=ident[:, :], compare_op=ALU.not_equal, fill=1.0, base=0,
                               pattern=[[-1, 128]], channel_multiplier=1).then_inc(consts_set, 1)
            pool.affine_select(out=shift_mask[:, :, :], in_=shift_mask[:, :, :], compare_op=ALU.not_equal, fill=-1.0,
                               base=-C, pattern=[[-1, TILES], [0, TROWS]], channel_multiplier=1).then_inc(consts_set, 1)

            def rstd_of(stat, which, stats_sem, count, eps_sem, rstd_sem, done):
                pool.wait_ge(stats_sem, count)
                pool.tensor_tensor(stat[0:N, 7:8], stat[0:N, 7:8], eps[0:N, :], ALU.add).then_inc(eps_sem, 1)
                pool.wait_ge(eps_sem, done)
                pool.tensor_tensor(rstd[0:N, which:which + 1], stat[0:N, 7:8], minus_half[0:N, :], ALU.pow).then_inc(rstd_sem, 1)

            def residual(b, par, fills):
                pool.wait_ge(x_loaded[par], 16 * fills)
                pool.tensor_tensor(x_res[0:N, par, :], x_in[0:N, par, :], bo_bc[0:N, :], ALU.add).then_inc(res_done, 1)

            rstd_of(stats[:, 0, :], 0, ln1_stats, 2, ln1_eps, ln1_rstd, 1)
            pool.wait_ge(gates_set, 2)
            pool.tensor_tensor(bo_bc[:, :], bo_bc[:, :], tanh_x[:, 0:1].to_broadcast([128, D]), ALU.mult).then_inc(tbo_done, 1)
            pool.wait_ge(tbo_done, 1)
            residual(0, 0, 1)

            def add_odd(t, c):
                r = CROWS[c]
                first = c == 3
                pool.wait_ge(probs_full, t.count(12, c + 1))
                if first and t.g >= 2:
                    pool.wait_ge(sum_v, t.count(6, -6))
                if not first:
                    pool.wait_ge(sum_p, t.count(5, (c - 3) // 2))
                left = probs[0:r, 1, :] if first else acc_p[0:r, t.g % 2, :]
                pool.tensor_tensor(acc_p[0:r, t.g % 2, :], left, probs[0:r, c % KS1, :], ALU.add).then_inc(sum_p, 1)

            def group(t):
                for c in range(CHUNKS):
                    if c == 2 and t.g % 2 == 0 and t.g + 2 < GROUPS:
                        rstd_of(stats[:, 0, :], 0, ln1_stats, 2 * t.batch(2), ln1_eps, ln1_rstd, t.batch(2))
                        residual(t.batch(1), t.parity(1), t.fills(1))
                    if c == 7 and t.g % 2 == 0 and t.g >= 2:
                        rstd_of(stats[:, 1, :], 1, ln2_stats, 2 * t.batch(), ln2_eps, ln2_rstd, t.batch())
                    if c >= 3 and c % 2:
                        add_odd(t, c)

            def finish(t):
                rstd_of(stats[:, 1, :], 1, ln2_stats, 2 * t.batch(), ln2_eps, ln2_rstd, t.batch())

            all_groups(pool, group, finish)

        @block.scalar
        def _(act):
            act.wait_ge(small_in, 48)
            act.activation(tanh_x[:, :], tanh_x[:, :], ACT.Tanh).then_inc(gates_set, 1)
            act.activation(tanh_f[:, :], tanh_f[:, :], ACT.Tanh).then_inc(gates_set, 1)

            def ring_use(t, key):
                kind, k = key
                if kind not in ("wqT", "wkT", "wvT", "A", "vo", "wT", "q", "ctx", "xT", "zT", "gate", "hT"):
                    return
                bank, n = t.ring(key)
                src, free = ring[:, bank, :], ring_free[bank]
                act.wait_ge(ring_full[bank], n)
                if kind == "wqT":
                    act.activation(wqT[:, 4 * k:4 * k + 4, :], src, ACT.Copy).then_inc(free, 1)
                elif kind == "wkT":
                    act.activation(wkT[:, :, :], src, ACT.Copy).then_inc(free, 1)
                elif kind == "wvT":
                    act.activation(wvT[:, :, 0, :], src, ACT.Copy)
                    act.activation(wvT[:, :, 1, :], src, ACT.Copy).then_inc(free, 1)
                elif kind == "A":
                    view = a_dup[:, :, :, :].rearrange("p (j r) i c -> p r i j c", r=2)
                    heads = src.rearrange("p (j c) -> p j c", c=C)
                    act.activation(view[:, k, 0], heads, ACT.Copy, scale=float(C) ** -0.5)
                    act.activation(view[:, k, 1], heads, ACT.Copy, scale=float(C) ** -0.5).then_inc(free, 1)
                elif kind == "vo":
                    view = vo[:, :, :].rearrange("p (j r) n -> p r j n", r=2)
                    act.activation(view[:, k % 2, 4 * (k // 2):4 * (k // 2) + 4], src.rearrange("p (j n) -> p j n", n=D), ACT.Copy).then_inc(free, 1)
                elif kind == "wT":
                    if k < 2:
                        act.activation((gateT, upT)[k][:, :], src[:, 0:F], ACT.Copy).then_inc(free, 1)
                    else:
                        rows = FT[k - 2]
                        act.activation(downT[0:rows, k - 2, :], src[0:rows, 0:D], ACT.Copy).then_inc(free, 1)
                elif kind == "q":
                    half = (t.g + 1) % 2
                    act.activation(q_hh[:, half, k * HALF:(k + 1) * HALF], src[:, 0:HALF], ACT.Copy).then_inc(q_hi_done, 1)
                elif kind == "ctx":
                    a, b = COFF[4 * k], COFF[4 * k + 4]
                    par = t.parity(1)
                    act.activation(k_h1[par][0:C, a:b], src[0:C, 0:b - a], ACT.Copy)
                    act.activation(k_hl[par][:, a:b], src[:, 0:b - a], ACT.Copy).then_inc(k_hi_done, 1)
                elif kind == "xT":
                    par = 0 if t.g < 0 else t.parity(1)
                    act.activation(xT[:, par, :], src[:, 0:N], ACT.Copy).then_inc(free, 1)
                elif kind == "zT":
                    act.activation(zT[:, :], src[:, 0:N], ACT.Copy).then_inc(free, 1)
                elif kind == "gate":
                    act.activation(e_gate[0:N, :], src[0:N, 0:F], ACT.Exp, scale=-1.0).then_inc(e_done, 1)
                elif kind == "hT":
                    act.activation(hT[:, 0:2, :], src[:, 0:2 * N], ACT.Copy)
                    act.activation(hT[0:FT[2], 2, :], src[0:FT[2], 2 * N:3 * N], ACT.Copy).then_inc(free, 1)

            for key in START:
                ring_use(Turn(-1), key)

            def copy_attn(t):
                act.wait_ge(pv_done, t.count(6, 0))
                act.activation(attn_sb[:, :].rearrange("p (k n) -> p k n", k=2), attn[:, :, 0:HALF], ACT.Copy).then_inc(attn_copied, 1)

            def exps(t, c):
                r = CROWS[c]
                act.wait_ge(scores_full, t.count(12, c + 1))
                old = c - KS1
                if t.g > 0 or old >= 0:
                    act.wait_ge(pv_done, t.count(6, old // 2 + 1))
                    if c % 2:
                        act.wait_ge(sum_p, t.count(5, 1 if old == 1 else (old - 1) // 2 if old > 1 else (old + 11) // 2 - 5))
                    else:
                        act.wait_ge(sum_v, t.count(6, 1 if old == 0 else old // 2 if old > 0 else (old + 12) // 2 - 6))
                act.activation(probs[0:r, c % KS1, :].rearrange("p (k n) -> p k n", k=2), scores[0:r, c % 2, :, 0:HALF],
                               ACT.Exp).then_inc(probs_full, 1)

            def group(t):
                for c in range(CHUNKS):
                    if c == 2 and t.g >= 1:
                        copy_attn(t)
                    exps(t, c)
                    for key in ring_keys(t.g, c):
                        ring_use(t, key)

            def finish(t):
                copy_attn(t)
                for key in FINISH:
                    ring_use(t, key)

            all_groups(act, group, finish)

        @block.tensor
        def _(pe):
            pe.wait_ge(consts_set, 7)
            pe.wait_ge(consts_v, 4)

            def ring_use(t, key):
                kind, k = key
                bank, n = t.ring(key)
                if t.g > 0 or n > 1:
                    pe.wait_ge(ring_free[bank], n - 1)
                dst = ring[:, bank, :]
                if kind == "wqT":
                    pe.wait_ge(wqk_in, 32)
                    for i in range(4):
                        mm = pe.transpose(dst[:, i * 128:(i + 1) * 128], wq[:, (4 * k + i) * 128:(4 * k + i + 1) * 128], ident[:, :])
                elif kind in ("wkT", "wvT"):
                    if kind == "wvT":
                        pe.wait_ge(wvo_in, 32)
                    w = wk if kind == "wkT" else wv
                    for j in range(HG):
                        mm = pe.transpose(dst[:, j * C:(j + 1) * C], w[:, j * 128:(j + 1) * 128], ident[0:C, 0:C])
                elif kind == "A":
                    wait_reads(pe, *[(t, used) for used in (("wqT", 0), ("wqT", 1), ("wkT", 0))], own=bank)
                    for j in range(HG):
                        mm = pe.matmul(dst[:, j * C:(j + 1) * C], wqT[64 * k:64 * k + C, j, :], wkT[64 * k:64 * k + C, j, :], start=True, stop=True)
                elif kind == "vo":
                    wait_reads(pe, (t, ("wvT", 0)), own=bank)
                    r = k % 2
                    for i in range(4):
                        j = 4 * (k // 2) + i
                        mm = pe.matmul(dst[:, i * D:(i + 1) * D], wvT[64 * r:64 * r + C, j, :, :].rearrange("p i c -> p (i c)"), wo[64 * r:64 * r + C, j, :], start=True, stop=True)
                elif kind == "wT":
                    pe.wait_ge(wq4, LINKS)
                    if k < 2:
                        for i in range(3):
                            mm = pe.transpose(dst[:, i * 128:i * 128 + FT[i]], w_fp4[0:FT[i], (3 * k + i) * D:(3 * k + i + 1) * D], ident[0:FT[i], 0:FT[i]])
                    else:
                        i = k - 2
                        mm = pe.transpose(dst[0:FT[i], 0:D], w_fp4[:, 6 * D + 128 * i:6 * D + 128 * i + FT[i]], ident[:, :])
                elif kind == "q":
                    if t.g % 2 and k == 0:
                        if t.g < 0:
                            wait_reads(pe, (t, ("xT", 0)), (t, ("A", 0)), (t, ("A", 1)), own=bank)
                        else:
                            wait_reads(pe, (t.before(), ("xT", 0)), own=bank)
                    par = (t.g + 1) // 2 % 2
                    for i in range(4):
                        h = HG * ((t.g + 1) % 2) + 4 * k + i
                        mm = pe.matmul(dst[:, i * N:(i + 1) * N], a_dup[:, h, :, :].rearrange("p i c -> p (i c)"), xT[:, par, :], start=True, stop=True)
                elif kind == "ctx":
                    par = t.parity(1)
                    if k == 0:
                        pe.wait_ge(ctx_loaded[par], 64 * t.fills(1))
                    for c in range(4 * k, 4 * k + 4):
                        r, a = CROWS[c], COFF[c] - COFF[4 * k]
                        mm = pe.transpose(dst[:, a:a + r], ctx_n[0:r, par, c, :, :].rearrange("p i d -> p (i d)"), ident[0:r, 0:r])
                elif kind == "xT":
                    pe.wait_ge(ln1_done, 1 if t.g < 0 else t.batch(2))
                    mm = pe.transpose(dst[:, 0:N], x_hat[0:N, :], ident[0:N, 0:N])
                elif kind == "max":
                    tile, part = k // 3, k % 3
                    if k == 0:
                        pe.wait_ge(q_hi_done, t.count(2, 4))
                        if t.g % 2:
                            wait_reads(pe, *[(t, ("ctx", used)) for used in range(3)], own=bank)
                    par = (t.g + 1) // 2 % 2
                    rows, a, b = TSIZE[tile], MAXC[part], MAXC[part + 1]
                    mm = pe.matmul(dst[0:rows, 0:b - a], q_hh[:, (t.g + 1) % 2, tile * TROWS:tile * TROWS + rows], k_hl[par][:, a:b], start=True, stop=True)
                elif kind == "shift":
                    pe.wait_ge(max_done, t.count(1, 2))
                    mm = pe.matmul(dst[C:C + TILES, 0:TROWS], maxes[0:TROWS, :], ident[0:TROWS, 0:TROWS], start=True, stop=True)
                elif kind == "sum":
                    pe.wait_ge(sum_v, t.count(6, 0))
                    for h in range(HG):
                        mm = pe.matmul(dst[0:N, h:h + 1], acc_v[0:CROWS[0], (t.g + 1) % 2, h * N:(h + 1) * N], ones[0:CROWS[0], 0:1], start=True, stop=True)
                elif kind == "proj":
                    if k == 0:
                        pe.wait_ge(attn_copied, t.count(1, 0))
                        if t.g == 1:
                            wait_reads(pe, *[(t.before(), ("vo", part)) for part in range(4)], own=bank)
                    for i in range(4):
                        h = 4 * k + i
                        mm = pe.matmul(dst[0:N, i * D:(i + 1) * D], attn_sb[:, h * N:(h + 1) * N], vo[:, HG * ((t.g + 1) % 2) + h, :], start=True, stop=True)
                elif kind == "zT":
                    pe.wait_ge(zq4, LINKS * t.batch())
                    mm = pe.transpose(dst[:, 0:N], z_fp4[0:N, :], ident[0:N, 0:N])
                elif kind in ("gate", "up"):
                    wait_reads(pe, (t, ("zT", 0)), own=bank)
                    mm = pe.matmul(dst[0:N, 0:F], zT[:, :], (gateT if kind == "gate" else upT)[:, :], start=True, stop=True)
                elif kind == "hT":
                    pe.wait_ge(hq4, LINKS * t.batch())
                    for i in range(3):
                        mm = pe.transpose(dst[0:FT[i], i * N:(i + 1) * N], h_fp4[0:N, 128 * i:128 * i + FT[i]], ident[0:N, 0:N])
                elif kind == "down":
                    wait_reads(pe, (t, ("hT", 0)), own=bank)
                    for i in range(3):
                        mm = pe.matmul(dst[0:N, 0:D], hT[0:FT[i], i, :], downT[0:FT[i], i, :], start=(i == 0), stop=(i == 2))
                mm.then_inc(ring_full[bank], 1)

            for key in START:
                ring_use(Turn(-1), key)

            def score_chunk(t, c):
                par, half, r, a = t.parity(), t.g % 2, CROWS[c], COFF[c]
                if c == 0:
                    wait_reads(pe, *[(t.before(), key) for key in (("q", 0), ("q", 1), ("shift", 0))])
                if t.g > 0 or c >= 2:
                    pe.wait_ge(probs_full, t.count(12, c - 1))
                for k in range(2):
                    cols = slice(k * HALF, (k + 1) * HALF)
                    dst = scores[0:r, c % 2, k, 0:HALF]
                    pe.matmul(dst, k_hl[par][:, a:a + r], q_hh[:, half, cols], start=True, stop=False)
                    mm = pe.matmul(dst, k_h1[par][0:C + TILES, a:a + r], q_ls[0:C + TILES, half, cols], start=False, stop=True)
                mm.then_inc(scores_full, 1)

            def attn_pair(t, j, back):
                par = (t.g - back) // 2 % 2
                pe.wait_ge(probs_full, t.count(12, 2 * j + 2 - 12 * back))
                if j == 0 and t.g >= 1:
                    pe.wait_ge(attn_copied, t.count(1, 0))
                for k in range(2):
                    for i in range(2):
                        c = 2 * j + i
                        r = CROWS[c]
                        mm = pe.matmul(attn[64 * i:64 * i + C, k, 0:HALF], ctx_n[0:r, par, c, 0, :], probs[0:r, c % KS1, k * HALF:(k + 1) * HALF],
                                       start=(j == 0), stop=(j == CHUNKS // 2 - 1))
                mm.then_inc(pv_done, 1)

            def group(t):
                for c in range(CHUNKS):
                    score_chunk(t, c)
                    for key in ring_keys(t.g, c):
                        ring_use(t, key)
                    if c == 1 and t.g >= 1:
                        attn_pair(t, CHUNKS // 2 - 1, 1)
                    elif c % 2 and c >= 3:
                        attn_pair(t, (c - 3) // 2, 0)

            def finish(t):
                attn_pair(t, CHUNKS // 2 - 1, 1)
                for key in FINISH:
                    ring_use(t, key)

            all_groups(pe, group, finish)

        @block.vector
        def _(dve):
            w3 = w_raw[:, 0:6 * D].rearrange("p (w k n) -> p w k n", w=2, k=3)
            dve.memset(w3[FT[2]:128, :, 2, :], 0.0).then_inc(consts_v, 1)
            for par in range(2):
                dve.memset(k_h1[par][C:C + TILES, :].bitcast(F32), 1.0).then_inc(consts_v, 1)
            dve.memset(max3[:, TILES - 1, :], 0.0).then_inc(consts_v, 1)

            def fp4(part, src, dst, mag, tmp, small, rows, links, base):
                n = src.shape[1] // BLOCK
                s3 = src.rearrange("p (n k) -> p n k", k=BLOCK)
                d3 = dst.rearrange("p (n k) -> p n k", k=BLOCK)
                m3 = mag.rearrange("p (n k) -> p n k", k=BLOCK)
                scale, inv = small[0:rows, 0, 0:n], small[0:rows, 1, 0:n]
                wide = lambda a: a.rearrange("p (n o) -> p n o", o=1).to_broadcast([rows, n, BLOCK])
                if part == 0:
                    dve.tensor_reduce(scale, s3, AX.X, ALU.max, apply_absolute_value=True).then_inc(links, 1)
                    dve.wait_ge(links, base + 1)
                    dve.tensor_scalar(scale, scale, 1.0 / 6.0, 1e-12, ALU.mult, ALU.max).then_inc(links, 1)
                    dve.wait_ge(links, base + 2)
                    dve.reciprocal(inv, scale).then_inc(links, 1)
                    dve.wait_ge(links, base + 3)
                if part == 1:
                    dve.tensor_tensor(m3, s3, wide(inv), ALU.mult).then_inc(links, 1)
                    dve.wait_ge(links, base + 4)
                    dve.tensor_scalar(mag.bitcast(I32), mag.bitcast(I32), 0x7FFFFFFF, None, ALU.bitwise_and).then_inc(links, 1)
                    dve.wait_ge(links, base + 5)
                if part == 2:
                    dve.tensor_scalar(tmp, mag, 5.0, 2.0, ALU.is_gt, ALU.mult).then_inc(links, 1)
                    dve.wait_ge(links, base + 6)
                    dve.scalar_tensor_tensor(out=tmp, in0=mag, scalar=3.5, in1=tmp, op0=ALU.is_gt, op1=ALU.add).then_inc(links, 1)
                    dve.wait_ge(links, base + 7)
                    dve.scalar_tensor_tensor(out=tmp, in0=mag, scalar=2.5, in1=tmp, op0=ALU.is_gt, op1=ALU.add).then_inc(links, 1)
                    dve.wait_ge(links, base + 8)
                if part == 3:
                    dve.tensor_scalar(dst, mag, 1.75, None, ALU.is_gt).then_inc(links, 1)
                    for i, mid in enumerate((1.25, 0.75, 0.25)):
                        dve.wait_ge(links, base + 9 + i)
                        dve.scalar_tensor_tensor(out=dst, in0=mag, scalar=mid, in1=dst, op0=ALU.is_gt, op1=ALU.add).then_inc(links, 1)
                    dve.wait_ge(links, base + 12)
                if part == 4:
                    dve.scalar_tensor_tensor(out=tmp, in0=dst, scalar=0.5, in1=tmp, op0=ALU.mult, op1=ALU.add).then_inc(links, 1)
                    dve.wait_ge(links, base + 13)
                    dve.scalar_tensor_tensor(out=tmp.bitcast(I32), in0=src.bitcast(I32), scalar=SGN, in1=tmp.bitcast(I32),
                                             op0=ALU.bitwise_and, op1=ALU.bitwise_or).then_inc(links, 1)
                    dve.wait_ge(links, base + 14)
                    dve.tensor_tensor(d3, tmp.rearrange("p (n k) -> p n k", k=BLOCK), wide(scale), ALU.mult).then_inc(links, 1)

            def weights_fp4(part):
                if part == 0:
                    dve.wait_ge(ffn_in, 80)
                fp4(part, w_raw[:, :], w_fp4[:, :], w_abs[:, :], w_t[:, :], w_small, 128, wq4, 0)

            def z_fp4_part(t, part):
                fp4(part, z[0:N, :], z_fp4[0:N, :], f_abs[0:N, 0:D], f_t[0:N, 0:D], f_small, N, zq4, LINKS * t.batch(-1))

            def h_fp4_part(t, part):
                if part == 0:
                    wait_reads(dve, (t, ("up", 0)))
                fp4(part, hid[0:N, :], h_fp4[0:N, :], f_abs[0:N, :], f_t[0:N, :], f_small, N, hq4, LINKS * t.batch(-1))

            def ln_stats(src, stat, done, before):
                dve.bn_stats(stat[0:N, 0:6], src).then_inc(done, 1)
                dve.wait_ge(done, before + 1)
                dve.memset(unused[0:1, :], 0.0)
                dve.bn_aggr(stat[0:N, 6:8], stat[0:N, 0:6]).then_inc(done, 1)

            def ln_apply(src, dst, stat, which, done):
                dve.tensor_scalar(dst, src, stat[0:N, 6:7], rstd[0:N, which:which + 1], ALU.subtract, ALU.mult).then_inc(done, 1)

            def ring_use(t, key):
                kind, k = key
                if kind not in ("q", "ctx", "max", "shift", "sum", "proj", "gate", "up", "down"):
                    return
                bank, n = t.ring(key)
                src, free = ring[:, bank, :], ring_free[bank]
                dve.wait_ge(ring_full[bank], n)
                if kind == "q":
                    half = (t.g + 1) % 2
                    dve.wait_ge(q_hi_done, t.count(2, 2 + k + 1))
                    cols = slice(k * HALF, (k + 1) * HALF)
                    dve.tensor_tensor(q_ls[0:C, half, cols], src[0:C, 0:HALF], q_hh[0:C, half, cols].bitcast(F32), ALU.subtract).then_inc(free, 1)
                elif kind == "ctx":
                    par = t.parity(1)
                    dve.wait_ge(k_hi_done, 3 * t.batch(1) + k + 1)
                    a, b = COFF[4 * k], COFF[4 * k + 4]
                    dve.tensor_tensor(k_hl[par][C:128, a:b], src[C:128, 0:b - a], k_hl[par][C:128, a:b].bitcast(F32), ALU.subtract).then_inc(free, 1)
                elif kind == "max":
                    tile, part = k // 3, k % 3
                    rows = TSIZE[tile]
                    dve.tensor_reduce(max3[0:rows, tile, part:part + 1], src[0:rows, 0:MAXC[part + 1] - MAXC[part]], AX.X, ALU.max).then_inc(free, 1)
                elif kind == "shift":
                    dve.tensor_tensor(q_ls[C:C + TILES, (t.g + 1) % 2, :].rearrange("p (k n) -> p k n", k=TILES), shift_mask[C:C + TILES, :, :],
                                      src[C:C + TILES, 0:TROWS].rearrange("p (o n) -> p o n", o=1).to_broadcast([TILES, TILES, TROWS]), ALU.mult).then_inc(free, 1)
                elif kind == "sum":
                    dve.reciprocal(rsum[0:N, :], src[0:N, 0:HG]).then_inc(norm_done, 1)
                    dve.wait_ge(norm_done, t.count(1, 0))
                    dve.tensor_scalar(rsum[0:N, :], rsum[0:N, :], tanh_x[0:N, :], None, ALU.mult).then_inc(free, 1)
                elif kind == "proj":
                    par = (t.g - 1) // 2 % 2
                    if k == 0:
                        if t.g % 2:
                            wait_reads(dve, (t, ("sum", 0)))
                            dve.wait_ge(res_done, t.batch(1))
                        else:
                            wait_reads(dve, (t, ("sum", 0)), (t.before(), ("proj", 1)))
                    else:
                        wait_reads(dve, (t, ("proj", 0)))
                    for i in range(4):
                        h = 4 * k + i
                        old = x_res if t.g % 2 and h == 0 else y
                        if i > 0:
                            dve.wait_ge(head_done, t.count(6, 3 * k + i - 6))
                        dve.scalar_tensor_tensor(out=y[0:N, par, :], in0=src[0:N, i * D:(i + 1) * D], scalar=rsum[0:N, h:h + 1],
                                                 in1=old[0:N, par, :], op0=ALU.mult, op1=ALU.add).then_inc(head_done if i < 3 else free, 1)
                elif kind == "gate":
                    done = 2 * t.batch(-1)
                    dve.wait_ge(e_done, t.batch())
                    dve.tensor_scalar(hid[0:N, :], e_gate[0:N, :], 1.0, None, ALU.add).then_inc(hid_done, 1)
                    dve.wait_ge(hid_done, done + 1)
                    dve.reciprocal(hid[0:N, :], hid[0:N, :]).then_inc(hid_done, 1)
                    dve.wait_ge(hid_done, done + 2)
                    dve.tensor_tensor(hid[0:N, :], src[0:N, 0:F], hid[0:N, :], ALU.mult).then_inc(free, 1)
                elif kind == "up":
                    wait_reads(dve, (t, ("gate", 0)))
                    dve.tensor_tensor(hid[0:N, :], src[0:N, 0:F], hid[0:N, :], ALU.mult).then_inc(free, 1)
                elif kind == "down":
                    par = t.parity(-1)
                    dve.wait_ge(stored[par], 16 * t.fills(-1))
                    dve.scalar_tensor_tensor(out=y_out[0:N, par, :], in0=src[0:N, 0:D], scalar=tanh_f[0:N, :], in1=y[0:N, par, :],
                                             op0=ALU.mult, op1=ALU.add).then_inc(free, 1)

            def add_even(t, c):
                r = CROWS[c]
                first = c == 2
                dve.wait_ge(probs_full, t.count(12, c + 1))
                if not first:
                    dve.wait_ge(sum_v, t.count(6, (c - 2) // 2))
                left = probs[0:r, 0, :] if first else acc_v[0:r, t.g % 2, :]
                dve.tensor_tensor(acc_v[0:r, t.g % 2, :], left, probs[0:r, c % KS1, :], ALU.add).then_inc(sum_v, 1)

            def add_last(t):
                r, par = CROWS[0], (t.g + 1) % 2
                dve.wait_ge(sum_p, t.count(5, 0))
                dve.wait_ge(sum_v, t.count(6, -1))
                dve.tensor_tensor(acc_v[0:r, par, :], acc_v[0:r, par, :], acc_p[0:r, par, :], ALU.add).then_inc(sum_v, 1)

            def max_tiles(t):
                wait_reads(dve, (t, ("max", 19)), (t, ("max", 20)))
                dve.tensor_reduce(maxes[0:TROWS, :], max3[0:TROWS, :, :], AX.X, ALU.max).then_inc(max_done, 1)

            def ln2(t, step):
                b = t.batch(-1)
                par = t.parity(-1)
                if step == 0:
                    wait_reads(dve, (t, ("proj", 1)))
                    ln_stats(y[0:N, par, :], stats[:, 1, :], ln2_stats, 2 * b)
                else:
                    dve.wait_ge(ln2_rstd, t.batch())
                    ln_apply(y[0:N, par, :], z[0:N, :], stats[:, 1, :], 1, ln2_done)
                    dve.wait_ge(ln2_done, t.batch())

            dve.wait_ge(x_loaded[0], 16)
            ln_stats(x_in[0:N, 0, :], stats[:, 0, :], ln1_stats, 0)
            dve.wait_ge(ln1_rstd, 1)
            ln_apply(x_in[0:N, 0, :], x_hat[0:N, :], stats[:, 0, :], 0, ln1_done)
            dve.wait_ge(consts_v, 4)
            dve.wait_ge(consts_set, 7)
            dve.wait_ge(gates_set, 2)
            for key in START:
                if key[0] == "shift":
                    max_tiles(Turn(-1))
                ring_use(Turn(-1), key)

            def group(t):
                for c in range(CHUNKS):
                    if c == 1 and t.g >= 1:
                        add_last(t)
                    if t.g % 2 == 0 and t.g + 2 < GROUPS:
                        par = t.parity(1)
                        if c == 1:
                            dve.wait_ge(x_loaded[par], 16 * t.fills(1))
                            ln_stats(x_in[0:N, par, :], stats[:, 0, :], ln1_stats, 2 * t.batch(1))
                        if c == 5:
                            dve.wait_ge(ln1_rstd, t.batch(2))
                            ln_apply(x_in[0:N, par, :], x_hat[0:N, :], stats[:, 0, :], 0, ln1_done)
                    if c == 10 and t.g + 1 < GROUPS:
                        max_tiles(t)
                    for key in ring_keys(t.g, c):
                        ring_use(t, key)
                    if c >= 3 and c % 2:
                        add_even(t, c - 1)
                    if t.g == 0 and 5 <= c <= 9:
                        weights_fp4(c - 5)
                    if t.g % 2 == 0 and t.g >= 2:
                        if c == 6:
                            ln2(t, 0)
                        if c == 7:
                            ln2(t, 1)
                        if 7 <= c <= 11:
                            z_fp4_part(t, c - 7)
                    if t.g % 2 and t.g >= 3 and 3 <= c <= 7:
                        h_fp4_part(t, c - 3)

            def finish(t):
                add_last(t)
                for key in FINISH:
                    if key[0] == "zT":
                        ln2(t, 0)
                        ln2(t, 1)
                        for part in range(5):
                            z_fp4_part(t, part)
                    if key[0] == "hT":
                        for part in range(5):
                            h_fp4_part(t, part)
                    ring_use(t, key)

            all_groups(dve, group, finish)


_INS = ["x", "ctx_512", "g_xattn", "g_ffn", "L0_xattn_Wq", "L0_xattn_Wk", "L0_xattn_Wv", "L0_xattn_Wo", "L0_xattn_bo",
        "L0_ffn_w_gate", "L0_ffn_w_up", "L0_ffn_w_down"]


def kernel(**inputs):
    import numpy as np
    import concourse.bacc as bacc
    from concourse.bass_utils import run_bass_kernel_spmd

    nc = bacc.Bacc("TRN2", target_bir_lowering=False, num_devices=1)
    arrays, args = {}, []
    for name in _INS:
        a = np.ascontiguousarray(inputs[name])
        arrays[f"in_{name}"] = a
        args.append(nc.dram_tensor(f"in_{name}", a.shape, mybir.dt.from_np(a.dtype), kind="ExternalInput").ap())
    args.append(nc.dram_tensor("out", (B, N, D), F32, kind="ExternalOutput").ap())
    xattn_ffn(nc, *args)
    r = run_bass_kernel_spmd(nc, [arrays], core_ids=[0])
    return r.results[0]["out"]
```
